# Optimizing a Trainium2 kernel written in Bass

```python
import numpy as np
import jax
import jax.numpy as jnp

def _softmax(x, axis=-1):
    return jax.nn.softmax(x, axis=axis)

def _gelu(x):
    return jax.nn.gelu(x, approximate=True)

def _silu(x):
    return jax.nn.silu(x)

def _sigmoid(x):
    return jax.nn.sigmoid(x)

def _layernorm(x, axis=-1, eps=1e-05):
    m = jnp.mean(x, axis=axis, keepdims=True)
    v = jnp.var(x, axis=axis, keepdims=True)
    return (x - m) / jnp.sqrt(v + eps)

def _scatter_add(tgt, idx, src, axis=0):
    return tgt.at[idx].add(src)

def _segment_sum(src, seg, n):
    return jax.ops.segment_sum(src, seg, n)
kernel_name = 'mk_seq_postln_d1_jaxref_r2_ef2616'

def setup_inputs(seed: int=0):
    np.random.seed(seed)
    _w = jnp.asarray

    def _L0_attn_setup():
        import jax, jax.numpy as jnp
        import numpy as np
        B, N, D = (4, 2048, 512)
        H, M = (16, 128)
        DH = D // H

        def _feature_map(t, omega):
            t_omega = jnp.einsum('bhnd,dm->bhnm', t, omega)
            norm_sq = 0.5 * jnp.sum(t * t, axis=-1, keepdims=True)
            return jnp.exp(t_omega - norm_sq)
        key = jax.random.key(seed)
        ks = jax.random.split(key, 6)
        x = jax.random.normal(ks[0], (B, N, D), dtype=jnp.float32)
        Wqkv = jax.random.normal(ks[1], (D, 3 * D), dtype=jnp.float32) * 0.02
        bqkv = jnp.zeros((3 * D,), dtype=jnp.float32)
        Wout = jax.random.normal(ks[2], (D, D), dtype=jnp.float32) * 0.02
        bout = jnp.zeros((D,), dtype=jnp.float32)
        omega = jax.random.normal(ks[3], (DH, M), dtype=jnp.float32)
        return {'x': x, 'Wqkv': Wqkv, 'bqkv': bqkv, 'Wout': Wout, 'bout': bout, 'omega': omega}
    _L0_attn_in = _L0_attn_setup()

    def _L0_ffn_setup():
        import jax, jax.numpy as jnp
        import numpy as np
        R = 64
        key = jax.random.key(seed)
        k1, k2, k3 = jax.random.split(key, 3)
        B, S, D_IN, D_OUT = (8, 2048, 512, 512)
        x = jax.random.normal(k1, (B, S, D_IN), dtype=jnp.float32)
        weight = jax.random.normal(k2, (D_OUT, D_IN), dtype=jnp.float32) * (1.0 / np.sqrt(D_IN))
        disha = jax.random.normal(k3, (R, D_OUT), dtype=jnp.float32) * 0.01
        return {'x': x, 'weight': weight, 'disha': disha}
    _L0_ffn_in = _L0_ffn_setup()
    _d = {'L0_attn_x': _L0_attn_in['x'], 'L0_attn_Wqkv': _L0_attn_in['Wqkv'], 'L0_attn_bqkv': _L0_attn_in['bqkv'], 'L0_attn_Wout': _L0_attn_in['Wout'], 'L0_attn_bout': _L0_attn_in['bout'], 'L0_attn_omega': _L0_attn_in['omega'], 'L0_ffn_weight': _L0_ffn_in['weight'], 'L0_ffn_disha': _L0_ffn_in['disha']}
    _x0 = _d['L0_attn_x']
    _d['L0_attn_x'] = jax.random.normal(jax.random.fold_in(jax.random.key(seed), 1), (8, 2048, 512), dtype=_x0.dtype)
    del _x0
    return _d

def reference(L0_attn_x, L0_attn_Wqkv, L0_attn_bqkv, L0_attn_Wout, L0_attn_bout, L0_attn_omega, L0_ffn_weight, L0_ffn_disha):

    def _L0_attn_ref(x, Wqkv, bqkv, Wout, bout, omega):
        import jax, jax.numpy as jnp
        import numpy as np
        B, N, D = (4, 2048, 512)
        H, M = (16, 128)
        DH = D // H

        def _feature_map(t, omega):
            t_omega = jnp.einsum('bhnd,dm->bhnm', t, omega)
            norm_sq = 0.5 * jnp.sum(t * t, axis=-1, keepdims=True)
            return jnp.exp(t_omega - norm_sq)
        b, n, d = x.shape
        qkv = x @ Wqkv + bqkv
        q, k, v = jnp.split(qkv, 3, axis=-1)

        def to_heads(t):
            return t.reshape(b, n, H, DH).transpose(0, 2, 1, 3)
        q, k, v = (to_heads(q), to_heads(k), to_heads(v))
        q_prime = _feature_map(q, omega)
        k_prime = _feature_map(k, omega)
        k_sum = jnp.sum(k_prime, axis=2)
        denominator = jnp.einsum('bhnm,bhm->bhn', q_prime, k_sum)[..., None]
        k_v = jnp.einsum('bhnm,bhnd->bhmd', k_prime, v)
        numerator = jnp.einsum('bhnm,bhmd->bhnd', q_prime, k_v)
        out = numerator / (denominator + 1e-06)
        out = out.transpose(0, 2, 1, 3).reshape(b, n, d)
        return out @ Wout + bout

    def _L0_ffn_ref(x, weight, disha):
        import jax, jax.numpy as jnp
        import numpy as np
        R = 64
        result = jnp.einsum('bsd,od->bso', x, weight)
        r = disha.shape[0]
        pooled = x.reshape(*x.shape[:-1], x.shape[-1] // r, r).sum(axis=-2)
        return result + pooled @ disha
    x = L0_attn_x
    x = _layernorm(x + _L0_attn_ref(x, L0_attn_Wqkv, L0_attn_bqkv, L0_attn_Wout, L0_attn_bout, L0_attn_omega), axis=-1)
    x = _layernorm(x + _L0_ffn_ref(x, L0_ffn_weight, L0_ffn_disha), axis=-1)
    return x

_drawn_inputs = setup_inputs


def setup_inputs(seed=0):
    import zlib

    import numpy as np

    out = dict(_drawn_inputs(seed))
    spreads = {'L0_attn_bqkv': (0.0, 0.1), 'L0_attn_bout': (0.0, 0.1)}
    factors = {}
    for name, (base, spread) in spreads.items():
        noise = np.random.default_rng([zlib.crc32(name.encode()), seed]).standard_normal(out[name].shape)
        drawn = base * np.exp(spread * noise) if base else spread * noise
        out[name] = jnp.asarray(drawn.astype(out[name].dtype))
    for name, factor in factors.items():
        out[name] = (out[name] * factor).astype(out[name].dtype)
    return out
```

```python
from contextlib import ExitStack

import concourse.bass as bass
from concourse import mybir

F32 = mybir.dt.float32
F16 = mybir.dt.float16
BF16 = mybir.dt.bfloat16
ALU = mybir.AluOpType
ACT = mybir.ActivationFunctionType

B, N, D = 8, 2048, 512
H, M = 16, 128
DH = D // H
P = 128
CHUNK = 512
CPB = N // CHUNK
TPC = CHUNK // P
KB = D // P
G = D // P
HPG = H // G
HALF = CHUNK // 2
W1 = DH + 1
WS = 16.0
NORM_MIN = -60000.0
STACK = 98
MOVES = 16 * (3 * HPG + 2 * G)
LN_EPS = 1e-5
DEN_EPS = 1e-6

ORDER = """
KP0. QF0 KP0 QF1 KP1. QF2 KP1 QF3 KP2. QF4 KP2 QF5 KP3. QF6 KP3 QF7
VP0. VP0 NM0 KN VP1. VP1 NM1 QP0. QP0 AT0 NM2 VP2. VP2 NM3 WO0. WO0 AT1 VP3. VP3
KF0 WO1. QF8 KF1 KV0 WO1 QF9 Y0 KF2 KV1 YT0 QP1. QF10 KF3 KV2 QP1 QF11 KF4 KV3 FF0. QF12 Y1 KF5 KV4 FF0 QF13
KF6 KV5 YT1 QP2. QF14 KF7 KV6 QP2 QF15 KF8 KV7 FF1. Z0 KF9 KV8 FF1 NM4 KF10 KV9 QP3. NM5 KF11 KV10 QP3 AT2 Z1
KF12 KV11 WO2. NM6 KF13 KV12 WO2 QN NM7 XS KF14 KV13 AT3 KF15 KV14 WO3. Y2 WO3 KV15 YT2 KFIN FF2. FF2 Y3 YT3 Z2 FF3. FF3 Z3
"""


def pieces(text):
    out = []
    for word in text.split():
        kind = word.rstrip(".0123456789")
        index = int(word[len(kind):].rstrip(".") or 0)
        halved = kind in ("KP", "VP", "QP", "WO", "FF")
        out.append((kind, index, "first" if word.endswith(".") else "last" if halved else "all"))
    return out


def later(order, kinds):
    keyed = [(n + kinds.get(p[0], 0) + (0.5 if p[0] in kinds else 0), p) for n, p in enumerate(order)]
    return [p for _, p in sorted(keyed, key=lambda x: x[0])]


PE_ORDER = pieces(ORDER)
ENDED = [p for p in PE_ORDER if p[2] != "first"]
ACT_ORDER = ENDED
DVE_ORDER = later(ENDED, {"KP": 1, "VP": 1, "QP": 1, "KF": 1, "QF": 1, "AT": 1, "YT": 1})
A_KINDS = ("KP", "VP", "KN", "KF", "KV", "KFIN", "XS")
Q_KINDS = ("QP", "QN")


def build(nc, xt, x, wqkv, bqk, bv, wout, bout, omega, wffn, disha, out):
    ctx = ExitStack()
    with ctx:
        def sb(name, shape, dt):
            return ctx.enter_context(nc.sbuf_tensor(name, shape, dt))

        def ps(name):
            return ctx.enter_context(nc.psum_tensor(name, [P, 512], F32))

        def sem(name):
            return ctx.enter_context(nc.semaphore(name))

        wqkv_hi, wqkv_lo = (sb(f"wqkv_{s}", [P, KB, 3 * D], F16) for s in ("hi", "lo"))
        wout_hi, wout_lo = (sb(f"wout_{s}", [P, KB, D], F16) for s in ("hi", "lo"))
        wffn_hi, wffn_lo = (sb(f"wffn_{s}", [P, KB, D], F16) for s in ("hi", "lo"))
        xt_f = sb("xt_f", [P, KB, CHUNK], F32)
        xt_hi, xt_lo = (sb(f"xt_{s}", [P, CPB, KB, CHUNK], F16) for s in ("hi", "lo"))
        t_hi = {s: sb(f"t_hi_{s}", [P, G, CHUNK], F16) for s in "kq"}
        t_lo = {s: sb(f"t_lo_{s}", [P, G, CHUNK], F16) for s in "kq"}
        half_norm = {s: sb(f"half_norm_{s}", [P, 2, CHUNK], F16) for s in "kq"}
        stack = {s: sb(f"stack_{s}", [P, HPG, G, CHUNK], F16) for s in "kq"}
        squares = sb("squares", [P, G, CHUNK], F32)
        k_feat = sb("k_feat", [P, 2, 512], F32)
        k_feat_lo = sb("k_feat_lo", [P, 2, 512], BF16)
        v_hi = sb("v_hi", [P, TPC, H, W1], F16)
        v_lo = sb("v_lo", [P, TPC, H, DH], F16)
        kv_f = sb("kv_f", [P, H, W1], F32)
        kv_hi = sb("kv_hi", [P, H, W1], BF16)
        kv_lo = sb("kv_lo", [P, H, W1], BF16)
        q_feat = sb("q_feat", [P, H, HALF], F32)
        q_feat_lo = sb("q_feat_lo", [P, H, HALF], BF16)
        den = sb("den", [P, 2, 8], F32)
        attn = sb("attn", [P, D], F32)
        at_hi, at_lo = (sb(f"at_{s}", [P, KB, P], F16) for s in ("hi", "lo"))
        yt_hi, yt_lo = (sb(f"yt_{s}", [P, KB, P], F16) for s in ("hi", "lo"))
        x_nat = sb("x_nat", [P, 2, D], F32)
        y = sb("y", [P, 2, D], F32)
        z = sb("z", [P, 2, D], F32)
        stats = sb("stats", [P, 2, 6], F32)
        mean_var = sb("mean_var", [P, 2, 2, 2], F32)
        rstd = sb("rstd", [P, 2, 2], F32)
        minus_half = sb("minus_half", [P, 1], F32)
        bias_qk = sb("bias_qk", [P, 2 * G], F32)
        bias_qk16 = sb("bias_qk16", [P, 2 * G], F32)
        bias_v16 = sb("bias_v16", [P, D], F32)
        bias_out = sb("bias_out", [P, D], F32)
        omega_f = sb("omega_f", [P, M], F32)
        omega_s = sb("omega_s", [P, M], F16)
        norm_w = sb("norm_w", [P, 32], F32)
        ident = sb("ident", [P, P], F32)

        w_stage = q_feat[:, :, :].rearrange("p h n -> p (h n)").rearrange("p (s n) -> p s n", s=2)
        k_feat_hi = k_feat[:, :, :].bitcast(BF16)[:, :, 1::2]
        q_feat_hi = q_feat[:, :, :].bitcast(BF16)[:, :, 1::2]

        kv_ps = [ps("kv_ps0"), ps("kv_ps1")]
        bank_a, bank_kf = ps("bank_a"), ps("bank_kf")
        bank_qf, bank_nm = ps("bank_qf"), ps("bank_nm")
        bank_x, bank_y = ps("bank_x"), ps("bank_y")

        def heads(bank):
            return bank[:, 0:8 * W1].rearrange("p (h w) -> p h w", w=W1)

        names = """const_loaded w_ready pool_const dve_const setup kp_done vp_done kn_done kf_done kv_done
            k_hi k_sq k_lo v_hi_done v_lo_done kn_hi kn_lo k_exp kfl kfin fin_a fin_b fin_c k_stacked
            qp_done qn_done qf_done nm_done at_done wo_done yt_done ff_done q_hi q_sq q_lo qn_hi qn_lo
            q_exp qfl q_stacked den_done rec_done normed at_hi_done at_lo_done yt_hi_done yt_lo_done
            xb_done st1 ag1 var1 rstd1 y_done r2_done st2 ag2 var2 rstd2 z_done
            xt_loaded xt_hi_done xt_lo_done dve_waited sp_waited""".split()
        S = {n: sem(n) for n in names}
        w_loaded = [sem("w_loaded0"), sem("w_loaded1")]
        x_loaded = [sem("x_loaded0"), sem("x_loaded1")]
        r1_done = [sem("r1_done0"), sem("r1_done1")]
        stored = [sem("stored0"), sem("stored1")]

        def wait(eng, name, value):
            if not isinstance(value, int) or value > 0:
                eng.wait_ge(S[name] if isinstance(name, str) else name, value)

        def runs(b, c, kind):
            if not isinstance(b, int):
                return True
            if kind in A_KINDS:
                return b < B
            if kind in Q_KINDS:
                return c == CPB - 1 if b == 0 else b < B or c < CPB - 1
            return b > 0

        def slots(eng, order, step):
            def iteration(b):
                for c in range(CPB):
                    for kind, i, what in order:
                        if runs(b, c, kind) and (kind != "KFIN" or c == CPB - 1):
                            step(b, c, kind, i, what)
            iteration(0)
            iteration(1)
            with eng.Fori(2, B) as b:
                iteration(b)
            iteration(B)

        SETUP_JOBS = KB + 2

        block = ctx.enter_context(nc.Block())

        @block.sync
        def _(sp):
            def load_xt(k):
                sp.dma_start(xt_f[:, :, :], xt[k, :, :, :]).then_inc(S["xt_loaded"], 16)

            for kb in range(2):
                sp.dma_start(w_stage[:, kb, 0:3 * D], wqkv[kb * P:(kb + 1) * P, :]).then_inc(w_loaded[kb], 16)
            load_xt(0)
            for r in range(3):
                sp.dma_start(omega_f[DH * r:DH * (r + 1), :], omega).then_inc(S["const_loaded"], 16)
            sp.dma_start(bias_qk[:, :], bqk).then_inc(S["const_loaded"], 16)
            sp.dma_start(bias_v16[:, :], bv.partition_broadcast(P)).then_inc(S["const_loaded"], 16)
            sp.dma_start(bias_out[:, :], bout.partition_broadcast(P)).then_inc(S["const_loaded"], 16)
            for r in range(2):
                sp.dma_start(attn[64 * r:64 * (r + 1), :], disha).then_inc(S["const_loaded"], 16)
            for n in range(2, SETUP_JOBS):
                sp.wait_ge(S["w_ready"], n - 1)
                src = (wqkv[n * P:(n + 1) * P, :] if n < KB else
                       (wout if n == KB else wffn).rearrange("(k p) n -> p k n", p=P))
                dst = w_stage[:, n % 2, 0:3 * D] if n < KB else \
                    w_stage[:, n % 2, :].rearrange("p (k n) -> p k n", k=KB)
                sp.dma_start(dst, src).then_inc(w_loaded[n % 2], 16)

            def carry():
                sp.sem_inc(S["sp_waited"], 1)

            def load_x(b, c, t):
                j, u = 4 * b - 4 + c, t % 2
                tile = sp.snap(TPC * j + t) if not isinstance(b, int) else TPC * j + t
                wait(sp, r1_done[u], 2 * j + t // 2)
                carry()
                sp.dma_start(x_nat[:, u, :], x[tile, :, :]).then_inc(x_loaded[u], 16)

            def store(b, c, t):
                j = 4 * b - 4 + c
                tile = sp.snap(TPC * j + t) if not isinstance(b, int) else TPC * j + t
                wait(sp, "z_done", TPC * j + t + 1)
                carry()
                sp.dma_start(out[tile, :, :], z[:, t % 2, :]).then_inc(stored[t % 2], 16)

            def stack_up(s, n, name):
                wait(sp, f"{s}_lo", G * (n + 1))
                carry()
                wait(sp, f"{s}f_done", 16 * n)
                for j in range(HPG):
                    for row, t in enumerate((t_hi[s], t_lo[s], t_hi[s])):
                        sp.dma_start(stack[s][DH * row:DH * (row + 1), j, :, :],
                                     t[DH * j:DH * (j + 1), :, :]).then_inc(S[name], 16)
                wait(sp, f"{s}n_lo", n + 1)
                for g in range(G):
                    for r in range(2):
                        sp.dma_start(stack[s][96 + r:97 + r, :, g, :],
                                     half_norm[s][32 * g:32 * g + HPG, r, :]).then_inc(S[name], 16)

            def step(b, c, kind, i):
                kA, j = 4 * b + c, 4 * b - 4 + c
                if kind == "load_xt":
                    n = (kA + 1) % (B * CPB)
                    n = n if isinstance(b, int) else sp.snap(n)
                    wait(sp, "xt_lo_done", kA + 1)
                    carry()
                    load_xt(n)
                if kind == "stack_k":
                    stack_up("k", kA, "k_stacked")
                if kind == "stack_q":
                    stack_up("q", j + 1, "q_stacked")
                if kind == "load_x":
                    load_x(b, c, i)
                if kind == "store":
                    store(b, c, i)

            like = {"load_xt": "KP", "stack_k": "KP", "stack_q": "QP"}
            order = [("load_xt", 0), ("load_x", 0), ("load_x", 1), ("stack_k", 0), ("load_x", 2), ("load_x", 3),
                     ("store", 0), ("store", 1), ("stack_q", 0), ("store", 2), ("store", 3)]

            def iteration(b):
                for c in range(CPB):
                    for kind, i in order:
                        if runs(b, c, like.get(kind, "NM")):
                            step(b, c, kind, i)
            iteration(0)
            iteration(1)
            with sp.Fori(2, B) as b:
                iteration(b)
            iteration(B)
            for u in range(2):
                sp.wait_ge(stored[u], 16 * B * N // P // 2)
            sp.wait_ge(S["xt_loaded"], 16 * (B * CPB + 1))

        @block.tensor
        def _(pe):
            pe.wait_ge(S["setup"], 1)
            pe.wait_ge(S["pool_const"], 2)

            FREED = {"KP": ("k_lo", 4), "VP": ("v_lo_done", 4), "KN": ("kn_lo", 1), "QP": ("q_lo", 4),
                     "QN": ("qn_lo", 1), "AT": ("at_lo_done", 4), "YT": ("yt_lo_done", 4)}

            def bank_free(b, c, kind, i, users):
                mine = [(k, n) for k, n, w in PE_ORDER if k in users and w != "first" and runs(b, c, k)]
                at = mine.index((kind, i))
                first = {"KP": 4 * b + c, "VP": 4 * b + c, "KN": 4 * b + c, "QP": 4 * b + c - 3,
                         "QN": 4 * b + c - 3, "AT": 4 * b + c - 4, "YT": 4 * b + c - 4}
                if at:
                    k, n = mine[at - 1]
                    name, per = FREED[k]
                    wait(pe, name, per * first[k] + n + 1)
                else:
                    for k in {"KP": ("VP",), "QP": ("YT", "QN"), "AT": ("YT", "QN")}[kind]:
                        name, per = FREED[k]
                        wait(pe, name, per * first[k])

            def twelve(bank, parts, what, done):
                at = [(kb, s, m) for kb in range(KB) for s, m in (("hi", "hi"), ("lo", "hi"), ("hi", "lo"))]
                for n in (range(0, 6) if what == "first" else range(6, 12)):
                    lhs, rhs = parts(*at[n])
                    last = nc.tensor.matmul(bank[:, :], lhs, rhs, start=n == 0, stop=n == 11)
                if what == "last":
                    last.then_inc(S[done], 1)

            w3, xt_p = {"hi": wqkv_hi, "lo": wqkv_lo}, {"hi": xt_hi, "lo": xt_lo}
            at_p, wo_p = {"hi": at_hi, "lo": at_lo}, {"hi": wout_hi, "lo": wout_lo}
            yt_p, wf_p = {"hi": yt_hi, "lo": yt_lo}, {"hi": wffn_hi, "lo": wffn_lo}

            def norms(done):
                for g in range(G):
                    last = nc.tensor.matmul(bank_x[32 * g:32 * (g + 1), :] if done == "qn_done" else
                                            bank_a[32 * g:32 * (g + 1), :],
                                            norm_w[:, :], squares[:, g, :], start=True, stop=True,
                                            skip_group_check=True)
                last.then_inc(S[done], 1)

            def step(b, c, kind, i, what):
                kA, j, jq = 4 * b + c, 4 * b - 4 + c, 4 * b - 3 + c
                if kind == "KP":
                    if what == "first":
                        if i == 0:
                            wait(pe, "xt_lo_done", kA + 1)
                        bank_free(b, c, kind, i, ("KP", "VP", "KN"))
                    twelve(bank_a, lambda kb, s, m: (w3[s][:, kb, D + P * i:D + P * (i + 1)],
                                                     xt_p[m][:, c, kb, :]), what, "kp_done")
                elif kind == "VP":
                    if what == "first":
                        bank_free(b, c, kind, i, ("KP", "VP", "KN"))
                    twelve(bank_a, lambda kb, s, m: (xt_p[s][:, c, kb, P * i:P * (i + 1)],
                                                     w3[m][:, kb, 2 * D:3 * D]), what, "vp_done")
                elif kind == "KN":
                    wait(pe, "k_sq", G * (kA + 1))
                    bank_free(b, c, kind, i, ("KP", "VP", "KN"))
                    norms("kn_done")
                elif kind == "KF":
                    t, g = i // G, i % G
                    if i == 0:
                        wait(pe, "k_stacked", MOVES * (kA + 1))
                    wait(pe, "k_exp", 16 * kA + i)
                    for jj in range(HPG):
                        last = nc.tensor.matmul(bank_kf[:, M * jj:M * (jj + 1)],
                                                stack["k"][0:STACK, jj, g, P * t:P * (t + 1)],
                                                omega_s[0:STACK, :], start=True, stop=True)
                    last.then_inc(S["kf_done"], 1)
                elif kind == "KV":
                    t, g = i // G, i % G
                    if i == 0:
                        wait(pe, "v_lo_done", TPC * (kA + 1))
                        if c == 0:
                            wait(pe, "kfin", b)
                    wait(pe, "kfl", 16 * kA + i + 1)
                    for jj in range(HPG):
                        h = HPG * g + jj
                        o = kv_ps[h // 8]
                        at = W1 * (h % 8)
                        hi = k_feat_hi[:, i % 2, M * jj:M * (jj + 1)]
                        lo = k_feat_lo[:, i % 2, M * jj:M * (jj + 1)]
                        end = c == CPB - 1 and t == TPC - 1 and h % 8 == 7
                        nc.tensor.matmul(o[:, at:at + W1], hi, v_hi[:, t, h, :],
                                         start=c == 0 and t == 0 and h % 8 == 0, stop=False,
                                         skip_group_check=True)
                        nc.tensor.matmul(o[:, at:at + DH], hi, v_lo[:, t, h, :], start=False, stop=False,
                                         skip_group_check=True)
                        last = nc.tensor.matmul(o[:, at:at + W1], lo, v_hi[:, t, h, :], start=False,
                                                stop=end, skip_group_check=True)
                    last.then_inc(S["kv_done"], 1)
                elif kind == "QP":
                    if what == "first":
                        bank_free(b, c, kind, i, ("QP", "QN", "AT", "YT"))
                    twelve(bank_x, lambda kb, s, m: (w3[s][:, kb, P * i:P * (i + 1)],
                                                     xt_p[m][:, (c + 1) % CPB, kb, :]), what, "qp_done")
                elif kind == "QN":
                    wait(pe, "q_sq", G * (jq + 1))
                    bank_free(b, c, kind, i, ("QP", "QN", "AT", "YT"))
                    norms("qn_done")
                elif kind == "QF":
                    half, pair = i // 8, i % 8
                    if i == 0:
                        wait(pe, "q_stacked", MOVES * (j + 1))
                    wait(pe, "q_exp", 16 * j + i)
                    for e in range(2):
                        hh = 2 * pair + e
                        last = nc.tensor.matmul(bank_qf[:, HALF * e:HALF * (e + 1)], omega_s[0:STACK, :],
                                                stack["q"][0:STACK, hh // G, hh % G,
                                                           HALF * half:HALF * (half + 1)],
                                                start=True, stop=True)
                    last.then_inc(S["qf_done"], 1)
                elif kind == "NM":
                    t, u = i // 2, i % 2
                    wait(pe, "qfl", 16 * j + 8 * (t // 2 + 1))
                    if i == 0:
                        wait(pe, "kfin", b)
                    wait(pe, "normed", 8 * j + i)
                    for hl in range(8):
                        h = 8 * u + hl
                        hh = G * (h % HPG) + h // HPG
                        pos = slice(P * (t % 2), P * (t % 2 + 1))
                        o = bank_nm[:, W1 * hl:W1 * (hl + 1)]
                        nc.tensor.matmul(o, q_feat_hi[:, hh, pos], kv_hi[:, h, :], start=True, stop=False)
                        nc.tensor.matmul(o, q_feat_hi[:, hh, pos], kv_lo[:, h, :], start=False, stop=False)
                        last = nc.tensor.matmul(o, q_feat_lo[:, hh, pos], kv_hi[:, h, :], start=False,
                                                stop=True)
                    last.then_inc(S["nm_done"], 1)
                elif kind in ("AT", "YT"):
                    if kind == "AT":
                        wait(pe, "normed", 8 * j + 2 * i + 2)
                    else:
                        wait(pe, "y_done", TPC * j + i + 1)
                    bank_free(b, c, kind, i, ("QP", "QN", "AT", "YT"))
                    src = attn[:, :] if kind == "AT" else y[:, i % 2, :]
                    for kb in range(KB):
                        last = nc.tensor.transpose(bank_x[:, P * kb:P * (kb + 1)],
                                                   src[:, P * kb:P * (kb + 1)], ident[:, :])
                    last.then_inc(S["at_done" if kind == "AT" else "yt_done"], 1)
                elif kind in ("WO", "FF"):
                    if what == "first":
                        wait(pe, "at_lo_done" if kind == "WO" else "yt_lo_done", TPC * j + i + 1)
                        mine = [(k, n) for k, n, w in PE_ORDER if k in ("WO", "FF") and w == "last"]
                        at = mine.index((kind, i))
                        k, n = mine[at - 1] if at else ("FF", -1)
                        if k == "WO":
                            wait(pe, r1_done[n % 2], 2 * j + n // 2 + 1)
                        else:
                            wait(pe, "r2_done", TPC * j + n + 1)
                    l, r = (at_p, wo_p) if kind == "WO" else (yt_p, wf_p)
                    twelve(bank_y, lambda kb, s, m: (l[s][:, kb, :], r[m][:, kb, :]), what,
                           "wo_done" if kind == "WO" else "ff_done")

            slots(pe, PE_ORDER, step)

        @block.scalar
        def _(act):
            act.wait_ge(S["setup"], 1)

            def project(s, bank, n, i, first_bias):
                wait(act, f"{s}p_done", G * n + i + 1)
                if i == 0:
                    wait(act, f"{s}_stacked", MOVES * n)
                m = first_bias + i
                nc.scalar.activation(t_hi[s][:, i, :], bank[:, :], ACT.Identity,
                                     bias=bias_qk16[:, m:m + 1]).then_inc(S[f"{s}_hi"], 1)

            def square(s, bank, i, first_bias):
                m = first_bias + i
                nc.scalar.activation(squares[:, i, :], bank[:, :], ACT.Square,
                                     bias=bias_qk[:, m:m + 1], scale=1.0 / WS).then_inc(S[f"{s}_sq"], 1)

            def step(b, c, kind, i, what):
                kA, j, jq = 4 * b + c, 4 * b - 4 + c, 4 * b - 3 + c
                if kind == "KP":
                    project("k", bank_a, kA, i, G)
                    if i == 0:
                        wait(act, "qn_done", jq)
                    square("k", bank_a, i, G)
                elif kind == "QP":
                    project("q", bank_x, jq, i, 0)
                    if i == 0:
                        wait(act, "kn_done", kA + 1 if runs(b, c, "KN") else B * CPB)
                    square("q", bank_x, i, 0)
                elif kind == "VP":
                    wait(act, "vp_done", TPC * kA + i + 1)
                    if i == 0:
                        wait(act, "kv_done", 16 * kA)
                    nc.scalar.activation(v_hi[:, i, :, 0:DH],
                                         bank_a[:, :].rearrange("p (h d) -> p h d", d=DH),
                                         ACT.Copy).then_inc(S["v_hi_done"], 1)
                elif kind == "KF":
                    wait(act, "kf_done", 16 * kA + i + 1)
                    wait(act, "kv_done", 16 * kA + i - 1)
                    nc.scalar.activation(k_feat[:, i % 2, :], bank_kf[:, :], ACT.Exp,
                                         scale=1.0 / WS).then_inc(S["k_exp"], 1)
                elif kind == "QF":
                    wait(act, "qf_done", 16 * j + i + 1)
                    if i % 8 == 0:
                        wait(act, "nm_done", 8 * j + i // 2)
                    pair = i % 8
                    nc.scalar.activation(q_feat[:, 2 * pair:2 * pair + 2, :],
                                         bank_qf[:, :].rearrange("p (e n) -> p e n", e=2), ACT.Exp,
                                         scale=1.0 / WS).then_inc(S["q_exp"], 1)
                elif kind == "AT":
                    wait(act, "at_done", TPC * j + i + 1)
                    wait(act, "wo_done", TPC * j + i)
                    nc.scalar.activation(at_hi[:, :, :], bank_x[:, :].rearrange("p (k n) -> p k n", k=KB),
                                         ACT.Copy).then_inc(S["at_hi_done"], 1)
                elif kind == "YT":
                    wait(act, "yt_done", TPC * j + i + 1)
                    wait(act, "ff_done", TPC * j + i)
                    nc.scalar.activation(yt_hi[:, :, :], bank_x[:, :].rearrange("p (k n) -> p k n", k=KB),
                                         ACT.Copy).then_inc(S["yt_hi_done"], 1)

            slots(act, ACT_ORDER, step)

        @block.vector
        def _(dve):
            v = nc.vector
            v.memset(norm_w[:, :], 0.0).then_inc(S["dve_const"], 1)
            v.memset(minus_half[:, :], -0.5).then_inc(S["dve_const"], 1)
            v.memset(v_hi[:, :, :, DH:W1], 1.0).then_inc(S["dve_const"], 1)
            v.memset(omega_s[96:98, :], WS).then_inc(S["dve_const"], 1)
            dve.wait_ge(S["dve_const"], 4)
            for j in range(HPG):
                v.memset(norm_w[DH * j:DH * (j + 1), j:j + 1], -0.5).then_inc(S["dve_const"], 1)
            dve.wait_ge(S["const_loaded"], 16 * 8)
            v.tensor_copy(omega_s[0:96, :], omega_f[0:96, :]).then_inc(S["dve_const"], 1)
            v.tensor_scalar(bias_qk16[:, :], bias_qk[:, :], WS, None, ALU.mult).then_inc(S["dve_const"], 1)
            v.tensor_scalar(bias_v16[:, :], bias_v16[:, :], WS, None, ALU.mult).then_inc(S["dve_const"], 1)
            dve.wait_ge(S["dve_const"], 11)
            v.tensor_tensor(omega_s[64:96, :], omega_f[64:96, :], omega_s[64:96, :],
                            ALU.subtract).then_inc(S["dve_const"], 1)

            def split_x(slot, k):
                wait(dve, "xt_loaded", 16 * (k + 1))
                v.tensor_copy(xt_hi[:, slot, :, :], xt_f[:, :, :]).then_inc(S["xt_hi_done"], 1)

            for n in range(SETUP_JOBS):
                dve.wait_ge(w_loaded[n % 2], 16 * (n // 2 + 1))
                src = w_stage[:, n % 2, 0:3 * D] if n < KB else w_stage[:, n % 2, :]
                if n < KB:
                    hi, lo = wqkv_hi[:, n, :], wqkv_lo[:, n, :]
                else:
                    hi, lo = (w[:, :, :].rearrange("p k n -> p (k n)")
                              for w in ((wout_hi, wout_lo) if n == KB else (wffn_hi, wffn_lo)))
                if n == KB + 1:
                    for kb in range(KB):
                        last = v.tensor_tensor(src[:, D * kb:D * (kb + 1)], src[:, D * kb:D * (kb + 1)],
                                               attn[:, :], ALU.add).then_inc(S["dve_const"], 1)
                    dve.wait_ge(S["dve_const"], 12 + n + KB)
                v.tensor_scalar(hi, src, WS, None, ALU.mult).then_inc(S["dve_const"], 1)
                dve.wait_ge(S["dve_const"], 12 + n + 1 + (KB if n == KB + 1 else 0))
                v.scalar_tensor_tensor(out=lo, in0=src, scalar=WS, in1=hi, op0=ALU.mult,
                                       op1=ALU.subtract).then_inc(S["w_ready"], 1)
            dve.wait_ge(S["w_ready"], SETUP_JOBS)
            split_x(0, 0)
            v.memset(den[:, :, :], 1.0).then_inc(S["setup"], 1)

            def stats_of(src, ln, u, before, value, s_name, a_name, v_name, n):
                dve.wait_ge(before, value)
                v.bn_stats(stats[:, ln, :], src).then_inc(S[s_name], 1)
                dve.wait_ge(S[s_name], n)
                dve.sem_inc(S["dve_waited"], 1)
                v.bn_aggr(mean_var[:, ln, u, :], stats[:, ln, :]).then_inc(S[a_name], 1)
                dve.wait_ge(S[a_name], n)
                v.tensor_scalar(mean_var[:, ln, u, 1:2], mean_var[:, ln, u, 1:2], LN_EPS, None,
                                ALU.add).then_inc(S[v_name], 1)

            def t_low(s, bank, n, i, first_bias):
                wait(dve, f"{s}_sq", G * n + i + 1)
                if i == 0:
                    wait(dve, f"{s}_stacked", MOVES * n)
                m = first_bias + i
                v.scalar_tensor_tensor(out=t_lo[s][:, i, :], in0=bank[:, :], scalar=bias_qk16[:, m:m + 1],
                                       in1=t_hi[s][:, i, :], op0=ALU.add,
                                       op1=ALU.subtract).then_inc(S[f"{s}_lo"], 1)

            def norm_parts(s, bank, n):
                wait(dve, f"{s}n_done", n + 1)
                wait(dve, f"{s}_stacked", MOVES * n)
                v.tensor_scalar(half_norm[s][:, 0, :], bank[:, :], NORM_MIN, None,
                                ALU.max).then_inc(S[f"{s}n_hi"], 1)
                wait(dve, f"{s}n_hi", n + 1)
                v.scalar_tensor_tensor(out=half_norm[s][:, 1, :], in0=bank[:, :], scalar=NORM_MIN,
                                       in1=half_norm[s][:, 0, :], op0=ALU.max,
                                       op1=ALU.subtract).then_inc(S[f"{s}n_lo"], 1)

            def step(b, c, kind, i, what):
                kA, j, jq = 4 * b + c, 4 * b - 4 + c, 4 * b - 3 + c
                n = TPC * j + i + 1
                u = i % 2
                if kind == "KP":
                    t_low("k", bank_a, kA, i, G)
                elif kind == "QP":
                    t_low("q", bank_x, jq, i, 0)
                elif kind == "KN":
                    norm_parts("k", bank_a, kA)
                elif kind == "QN":
                    norm_parts("q", bank_x, jq)
                elif kind == "VP":
                    wait(dve, "v_hi_done", TPC * kA + i + 1)
                    if i == 0:
                        wait(dve, "kv_done", 16 * kA)
                    v.tensor_tensor(v_lo[:, i, :, :], bank_a[:, :].rearrange("p (h d) -> p h d", d=DH),
                                    v_hi[:, i, :, 0:DH], ALU.subtract).then_inc(S["v_lo_done"], 1)
                elif kind == "KF":
                    wait(dve, "k_exp", 16 * kA + i + 1)
                    wait(dve, "kv_done", 16 * kA + i - 1)
                    v.tensor_tensor(k_feat_lo[:, u, :], k_feat[:, u, :], k_feat_hi[:, u, :],
                                    ALU.subtract).then_inc(S["kfl"], 1)
                elif kind == "QF":
                    wait(dve, "q_exp", 16 * j + i + 1)
                    if i % 8 == 0:
                        wait(dve, "nm_done", 8 * j + i // 2)
                    at = slice(2 * (i % 8), 2 * (i % 8) + 2)
                    v.tensor_tensor(q_feat_lo[:, at, :], q_feat[:, at, :], q_feat_hi[:, at, :],
                                    ALU.subtract).then_inc(S["qfl"], 1)
                elif kind == "KFIN":
                    wait(dve, "kv_done", 16 * (kA + 1))
                    wait(dve, "nm_done", 8 * (j + 1))
                    for uu in range(2):
                        src = heads(kv_ps[uu])
                        dst = kv_f[:, 8 * uu:8 * uu + 8, :]
                        v.tensor_tensor(dst[:, :, 0:DH],
                                        bias_v16[:, 256 * uu:256 * (uu + 1)].rearrange("p (h d) -> p h d", d=DH),
                                        src[:, :, DH:W1].to_broadcast([P, 8, DH]),
                                        ALU.mult).then_inc(S["fin_a"], 1)
                        v.tensor_copy(dst[:, :, DH:W1], src[:, :, DH:W1]).then_inc(S["fin_a"], 1)
                    wait(dve, "fin_a", 4 * b + 4)
                    for uu in range(2):
                        dst = kv_f[:, 8 * uu:8 * uu + 8, 0:DH]
                        v.tensor_tensor(dst, heads(kv_ps[uu])[:, :, 0:DH], dst, ALU.add).then_inc(S["fin_b"], 1)
                    wait(dve, "fin_b", 2 * b + 2)
                    v.tensor_copy(kv_hi[:, :, :], kv_f[:, :, :]).then_inc(S["fin_c"], 1)
                    wait(dve, "fin_c", b + 1)
                    v.tensor_tensor(kv_lo[:, :, :], kv_f[:, :, :], kv_hi[:, :, :],
                                    ALU.subtract).then_inc(S["kfin"], 1)
                elif kind == "NM":
                    t, uu = i // 2, i % 2
                    m = 8 * j + i + 1
                    wait(dve, "nm_done", m)
                    src = heads(bank_nm)
                    v.tensor_scalar(den[:, 0, :], src[:, :, DH:W1].rearrange("p h o -> p (h o)"), DEN_EPS,
                                    None, ALU.add).then_inc(S["den_done"], 1)
                    wait(dve, "den_done", m)
                    v.reciprocal(den[:, 1, :], den[:, 0, :]).then_inc(S["rec_done"], 1)
                    wait(dve, "rec_done", m)
                    if uu == 0:
                        wait(dve, "at_done", TPC * j + t)
                    v.tensor_tensor(attn[:, 256 * uu:256 * (uu + 1)].rearrange("p (h d) -> p h d", d=DH),
                                    src[:, :, 0:DH],
                                    den[:, 1, :].rearrange("p (h o) -> p h o", o=1).to_broadcast([P, 8, DH]),
                                    ALU.mult).then_inc(S["normed"], 1)
                elif kind == "AT":
                    wait(dve, "at_hi_done", n)
                    v.tensor_tensor(at_lo[:, :, :], bank_x[:, :].rearrange("p (k n) -> p k n", k=KB),
                                    at_hi[:, :, :], ALU.subtract).then_inc(S["at_lo_done"], 1)
                elif kind == "YT":
                    wait(dve, "yt_hi_done", n)
                    v.tensor_tensor(yt_lo[:, :, :], bank_x[:, :].rearrange("p (k n) -> p k n", k=KB),
                                    yt_hi[:, :, :], ALU.subtract).then_inc(S["yt_lo_done"], 1)
                elif kind == "WO":
                    wait(dve, "wo_done", n)
                    wait(dve, "xb_done", n)
                    v.scalar_tensor_tensor(out=y[:, u, :], in0=bank_y[:, :], scalar=1.0 / WS / WS,
                                           in1=x_nat[:, u, :], op0=ALU.mult,
                                           op1=ALU.add).then_inc(r1_done[u], 1)
                    stats_of(y[:, u, :], 0, u, r1_done[u], 2 * j + i // 2 + 1, "st1", "ag1", "var1", n)
                elif kind == "Y":
                    wait(dve, "rstd1", n)
                    v.tensor_scalar(y[:, u, :], y[:, u, :], mean_var[:, 0, u, 0:1], rstd[:, 0, u:u + 1],
                                    ALU.subtract, ALU.mult).then_inc(S["y_done"], 1)
                elif kind == "FF":
                    wait(dve, "ff_done", n)
                    wait(dve, stored[u], 16 * (2 * j + i // 2))
                    v.scalar_tensor_tensor(out=z[:, u, :], in0=bank_y[:, :], scalar=1.0 / WS,
                                           in1=y[:, u, :], op0=ALU.mult,
                                           op1=ALU.add).then_inc(S["r2_done"], 1)
                    stats_of(z[:, u, :], 1, u, S["r2_done"], n, "st2", "ag2", "var2", n)
                elif kind == "Z":
                    wait(dve, "rstd2", n)
                    v.tensor_scalar(z[:, u, :], z[:, u, :], mean_var[:, 1, u, 0:1], rstd[:, 1, u:u + 1],
                                    ALU.subtract, ALU.mult).then_inc(S["z_done"], 1)
                elif kind == "XS":
                    wait(dve, "qp_done", G * (kA - 2))
                    split_x((c + 1) % CPB, kA + 1)

            slots(dve, DVE_ORDER, step)

        @block.gpsimd
        def _(pool):
            nc.gpsimd.memset(ident[:, :], 0.0).then_inc(S["pool_const"], 1)
            pool.wait_ge(S["pool_const"], 1)
            nc.gpsimd.affine_select(out=ident[:, :], in_=ident[:, :], compare_op=ALU.not_equal, fill=1.0,
                                    base=0, pattern=[[-1, P]], channel_multiplier=1
                                    ).then_inc(S["pool_const"], 1)
            pool.wait_ge(S["dve_const"], 4)
            pool.wait_ge(S["const_loaded"], 16 * 8)

            def split_x_low(slot, k):
                wait(pool, "xt_hi_done", k + 1)
                for kb in range(KB):
                    last = nc.gpsimd.tensor_tensor(xt_lo[:, slot, kb, :], xt_f[:, kb, :],
                                                   xt_hi[:, slot, kb, :], ALU.subtract)
                last.then_inc(S["xt_lo_done"], 1)

            def add_bias(j, t):
                wait(pool, x_loaded[t % 2], 16 * (2 * j + t // 2 + 1))
                nc.gpsimd.tensor_tensor(x_nat[:, t % 2, :], x_nat[:, t % 2, :], bias_out[:, :],
                                        ALU.add).then_inc(S["xb_done"], 1)

            split_x_low(0, 0)

            def step(b, c, kind, i, what):
                kA, j = 4 * b + c, 4 * b - 4 + c
                if kind in ("WO", "FF"):
                    ln = 0 if kind == "WO" else 1
                    wait(pool, f"var{ln + 1}", TPC * j + i + 1)
                    nc.gpsimd.tensor_tensor(rstd[:, ln, i % 2:i % 2 + 1], mean_var[:, ln, i % 2, 1:2],
                                            minus_half[:, :], ALU.pow).then_inc(S[f"rstd{ln + 1}"], 1)
                    if kind == "WO" and i < 2:
                        add_bias(j, i + 2)
                elif kind == "QF" and i in (0, 1):
                    add_bias(j, i)
                elif kind == "XS":
                    split_x_low((c + 1) % CPB, kA + 1)

            slots(pool, ENDED, step)


_OUT_SHAPE = (B, N, D)


def kernel(**inputs):
    import numpy as _np
    import concourse.bacc as _bacc
    from concourse.bass_utils import run_bass_kernel_spmd as _run

    x = _np.ascontiguousarray(inputs["L0_attn_x"])
    n_chunks, n_tiles = B * N // CHUNK, B * N // P
    bqkv = _np.ascontiguousarray(inputs["L0_attn_bqkv"])
    arrays = {
        "xt": _np.ascontiguousarray(x.reshape(n_chunks, CHUNK, KB, P).transpose(0, 3, 2, 1)),
        "x": x.reshape(n_tiles, P, D),
        "wqkv": _np.ascontiguousarray(inputs["L0_attn_Wqkv"]),
        "bqk": _np.ascontiguousarray(bqkv[:2 * D].reshape(2 * G, P).T),
        "bv": _np.ascontiguousarray(bqkv[2 * D:]),
        "wout": _np.ascontiguousarray(inputs["L0_attn_Wout"]),
        "bout": _np.ascontiguousarray(inputs["L0_attn_bout"]),
        "omega": _np.ascontiguousarray(inputs["L0_attn_omega"]),
        "wffn": _np.ascontiguousarray(_np.asarray(inputs["L0_ffn_weight"]).T),
        "disha": _np.ascontiguousarray(inputs["L0_ffn_disha"]),
    }
    nc = _bacc.Bacc("TRN2", target_bir_lowering=False, num_devices=1)
    args = [nc.dram_tensor(n, a.shape, mybir.dt.from_np(a.dtype), kind="ExternalInput").ap()
            for n, a in arrays.items()]
    out = nc.dram_tensor("out", (n_tiles, P, D), F32, kind="ExternalOutput").ap()
    build(nc, *args, out)
    r = _run(nc, [arrays], core_ids=[0])
    return r.results[0]["out"].reshape(_OUT_SHAPE)
```

```python
from contextlib import ExitStack

import concourse.bass as bass
from concourse import mybir

F32 = mybir.dt.float32
F16 = mybir.dt.float16
BF16 = mybir.dt.bfloat16
ALU = mybir.AluOpType
ACT = mybir.ActivationFunctionType

B, N, D = 8, 2048, 512
H, M = 16, 128
DH = D // H
P = 128
CHUNK = 512
CPB = N // CHUNK
TPC = CHUNK // P
KB = D // P
G = D // P
HPG = H // G
HALF = CHUNK // 2
W1 = DH + 1
WS = 16.0
NORM_MIN = -60000.0
STACK = 98
MOVES = 16 * (3 * HPG + 2 * G)
LN_EPS = 1e-5
DEN_EPS = 1e-6

ORDER = """
KP0. KF7' KV6' QN' KP0 KF8'
FF1'. KV7' FF1' AT2' Z0' NM6'
KP1. KF9' KV8' KP1 NM7'
WO2'. KF10' KV9' WO2' Z1'
KP2. AT3' QF0 KP2 KF11' KV10'
QP0. KF12' KV11' QP0 QF1
WO3'. Y2' KF13' KV12' WO3' YT2' QF2
KP3. QF3 KF14' KV13' KP3 QF4
QP1. QF5 KF15' KV14' QP1 QF6
FF2'. Y3' KN KV15' KFIN' FF2' YT3' QF7
VP0. Z2' VP0
FF3'. NM0 FF3' NM1
VP1. AT0 NM2 VP1 Z3'
WO0. NM3 WO0 KF0
QP2. QF8 KF1 KV0 QP2 QF9
VP2. AT1 QF10 KF2 KV1 VP2 Y0 QF11
WO1. YT0 QF12 KF3 KV2 WO1 QF13
QP3. QF14 KF4 KV3 QP3 XS QF15
VP3. Y1 KF5 KV4 VP3 NM4
FF0. YT1 KF6 KV5 FF0 NM5
"""


def pieces(text):
    out = []
    for word in text.split():
        kind = word.rstrip(".'0123456789")
        index = int(word[len(kind):].rstrip(".'") or 0)
        halved = kind in ("KP", "VP", "QP", "WO", "FF")
        out.append((kind, index, "first" if word.endswith(".") else "last" if halved else "all",
                    int("'" in word)))
    return out


def later(order, kinds):
    keyed = [(n + kinds.get(p[0], 0) + (0.5 if p[0] in kinds else 0), p) for n, p in enumerate(order)]
    return [p for _, p in sorted(keyed, key=lambda x: x[0])]


PE_ORDER = pieces(ORDER)
ENDED = [p for p in PE_ORDER if p[2] != "first"]
ACT_ORDER = ENDED
DVE_ORDER = later(ENDED, {"KP": 1, "VP": 1, "QP": 1, "KF": 1, "QF": 1, "AT": 1, "YT": 1, "KN": 1})
SP_ORDER = pieces("""
XT NRQ' ST0' LX0 ST1' LX1 STK NRK ST2' LX2 ST3' LX3 STQ
""")
A_KINDS = ("KP", "VP", "KN", "KF", "KV", "KFIN", "XS", "XT", "STK", "NRK")
Q_KINDS = ("QP", "QN", "STQ", "NRQ")


def build(nc, xt, x, wqkv, bqk, bv, wout, bout, omega, wffn, disha, out):
    ctx = ExitStack()
    with ctx:
        def sb(name, shape, dt):
            return ctx.enter_context(nc.sbuf_tensor(name, shape, dt))

        def ps(name):
            return ctx.enter_context(nc.psum_tensor(name, [P, 512], F32))

        def sem(name):
            return ctx.enter_context(nc.semaphore(name))

        wqkv_hi, wqkv_lo = (sb(f"wqkv_{s}", [P, KB, 3 * D], F16) for s in ("hi", "lo"))
        wout_hi, wout_lo = (sb(f"wout_{s}", [P, KB, D], F16) for s in ("hi", "lo"))
        wffn_hi, wffn_lo = (sb(f"wffn_{s}", [P, KB, D], F16) for s in ("hi", "lo"))
        xt_f = sb("xt_f", [P, KB, CHUNK], F32)
        xt_hi, xt_lo = (sb(f"xt_{s}", [P, CPB, KB, CHUNK], F16) for s in ("hi", "lo"))
        t_hi = {s: sb(f"t_hi_{s}", [P, G, CHUNK], F16) for s in "kq"}
        t_lo = {s: sb(f"t_lo_{s}", [P, G, CHUNK], F16) for s in "kq"}
        half_norm = sb("half_norm", [P, 2, CHUNK], F16)
        stack = {s: sb(f"stack_{s}", [P, HPG, G, CHUNK], F16) for s in "kq"}
        squares = {s: sb(f"squares_{s}", [P, G, CHUNK], F32) for s in "kq"}
        k_feat = sb("k_feat", [P, 2, 512], F32)
        k_feat_lo = sb("k_feat_lo", [P, 2, 512], BF16)
        v_hi = sb("v_hi", [P, TPC, H, W1], F16)
        v_lo = sb("v_lo", [P, TPC, H, DH], F16)
        kv_hi = sb("kv_hi", [P, H, W1], BF16)
        kv_lo = sb("kv_lo", [P, H, W1], BF16)
        q_feat = sb("q_feat", [P, H, HALF], F32)
        q_feat_lo = sb("q_feat_lo", [P, H, HALF], BF16)
        den = sb("den", [P, 2, 8], F32)
        attn = sb("attn", [P, D], F32)
        at_hi, at_lo = (sb(f"at_{s}", [P, KB, P], F16) for s in ("hi", "lo"))
        yt_hi, yt_lo = (sb(f"yt_{s}", [P, 2, KB, P], F16) for s in ("hi", "lo"))
        rows = sb("rows", [P, TPC, D], F32)
        stats = sb("stats", [P, 2, 6], F32)
        mean_var = sb("mean_var", [P, 2, 2, 2], F32)
        rstd = sb("rstd", [P, 2, 2], F32)
        minus_half = sb("minus_half", [P, 1], F32)
        bias_qk = sb("bias_qk", [P, 2 * G], F32)
        bias_qk16 = sb("bias_qk16", [P, 2 * G], F32)
        bias_v16 = sb("bias_v16", [P, D], F32)
        bias_out = sb("bias_out", [P, D], F32)
        omega_f = sb("omega_f", [P, M], F32)
        omega_s = sb("omega_s", [P, M], F16)
        norm_w = sb("norm_w", [P, 32], F32)
        ident = sb("ident", [P, P], F32)

        w_stage = q_feat[:, :, :].rearrange("p h n -> p (h n)").rearrange("p (s n) -> p s n", s=2)
        kv_f = squares["k"][:, :, :].rearrange("p g n -> p (g n)")[:, 0:H * W1].rearrange(
            "p (h w) -> p h w", w=W1)
        k_feat_hi = k_feat[:, :, :].bitcast(BF16)[:, :, 1::2]
        q_feat_hi = q_feat[:, :, :].bitcast(BF16)[:, :, 1::2]

        kv_ps = [ps("kv_ps0"), ps("kv_ps1")]
        bank_a, bank_kf = ps("bank_a"), ps("bank_kf")
        bank_qf, bank_nm = ps("bank_qf"), ps("bank_nm")
        bank_x, bank_y = ps("bank_x"), ps("bank_y")

        def heads(bank):
            return bank[:, 0:8 * W1].rearrange("p (h w) -> p h w", w=W1)

        names = """const_loaded w_ready pool_const dve_const setup kp_done vp_done kn_done kf_done kv_done
            k_hi k_sq k_lo v_hi_done v_lo_done kn_hi kn_lo k_exp kfl kfin fin_a fin_b fin_c k_stacked
            qp_done qn_done qf_done nm_done at_done wo_done yt_done ff_done q_hi q_sq q_lo qn_hi qn_lo
            q_exp qfl q_stacked den_done rec_done normed at_hi_done at_lo_done yt_hi_done yt_lo_done
            xb_done r1_done st1 ag1 var1 rstd1 y_done r2_done st2 ag2 var2 rstd2 z_done
            xt_loaded xt_hi_done xt_lo_done dve_waited sp_waited""".split()
        S = {n: sem(n) for n in names}
        w_loaded = [sem("w_loaded0"), sem("w_loaded1")]
        x_loaded = [sem(f"x_loaded{t}") for t in range(TPC)]
        stored = [sem(f"stored{t}") for t in range(TPC)]

        def wait(eng, name, value):
            if not isinstance(value, int) or value > 0:
                eng.wait_ge(S[name] if isinstance(name, str) else name, value)

        def chunk_of(b, c, kind, back=0):
            first = 0 if kind in A_KINDS else CPB - 1 if kind in Q_KINDS else CPB
            return CPB * b + c - back - first

        def runs(b, c, kind, back=0):
            return not isinstance(b, int) or 0 <= chunk_of(b, c, kind, back) < B * CPB

        def slots(eng, order, step):
            def slot(b, c):
                for kind, i, what, back in order:
                    if runs(b, c, kind, back) and (kind != "KFIN" or (c - back) % CPB == CPB - 1):
                        step(b, c - back, kind, i, what)

            def iteration(b):
                for c in range(CPB):
                    slot(b, c)
            iteration(0)
            iteration(1)
            with eng.Fori(2, B) as b:
                iteration(b)
            iteration(B)
            slot(B, CPB)

        SETUP_JOBS = KB + 2

        block = ctx.enter_context(nc.Block())

        @block.sync
        def _(sp):
            def load_xt(k):
                sp.dma_start(xt_f[:, :, :], xt[k, :, :, :]).then_inc(S["xt_loaded"], 16)

            for kb in range(2):
                sp.dma_start(w_stage[:, kb, 0:3 * D], wqkv[kb * P:(kb + 1) * P, :]).then_inc(w_loaded[kb], 16)
            load_xt(0)
            for r in range(3):
                sp.dma_start(omega_f[DH * r:DH * (r + 1), :], omega).then_inc(S["const_loaded"], 16)
            sp.dma_start(bias_qk[:, :], bqk).then_inc(S["const_loaded"], 16)
            sp.dma_start(bias_v16[:, :], bv.partition_broadcast(P)).then_inc(S["const_loaded"], 16)
            sp.dma_start(bias_out[:, :], bout.partition_broadcast(P)).then_inc(S["const_loaded"], 16)
            for r in range(2):
                sp.dma_start(attn[64 * r:64 * (r + 1), :], disha).then_inc(S["const_loaded"], 16)
            for n in range(2, SETUP_JOBS):
                sp.wait_ge(S["w_ready"], n - 1)
                src = (wqkv[n * P:(n + 1) * P, :] if n < KB else
                       (wout if n == KB else wffn).rearrange("(k p) n -> p k n", p=P))
                dst = w_stage[:, n % 2, 0:3 * D] if n < KB else \
                    w_stage[:, n % 2, :].rearrange("p (k n) -> p k n", k=KB)
                sp.dma_start(dst, src).then_inc(w_loaded[n % 2], 16)

            def carry():
                sp.sem_inc(S["sp_waited"], 1)

            def load_x(b, c, t, n):
                tile = TPC * n + t
                wait(sp, stored[t], 16 * n)
                carry()
                sp.dma_start(rows[:, t, :], x[tile if isinstance(b, int) else sp.snap(tile), :, :]
                             ).then_inc(x_loaded[t], 16)

            def store(b, c, t, n):
                tile = TPC * n + t
                wait(sp, "z_done", tile + 1)
                carry()
                sp.dma_start(out[tile if isinstance(b, int) else sp.snap(tile), :, :], rows[:, t, :]
                             ).then_inc(stored[t], 16)

            def stack_up(s, n, name):
                wait(sp, f"{s}_lo", G * (n + 1))
                carry()
                wait(sp, f"{s}f_done", 16 * n)
                for j in range(HPG):
                    for row, t in enumerate((t_hi[s], t_lo[s], t_hi[s])):
                        sp.dma_start(stack[s][DH * row:DH * (row + 1), j, :, :],
                                     t[DH * j:DH * (j + 1), :, :]).then_inc(S[name], 16)

            def stack_norms(s, n, name):
                wait(sp, f"{s}n_lo", n + 1)
                for g in range(G):
                    for r in range(2):
                        sp.dma_start(stack[s][96 + r:97 + r, :, g, :],
                                     half_norm[32 * g:32 * g + HPG, r, :]).then_inc(S[name], 16)

            def step(b, c, kind, i, what):
                kA, j, jq = 4 * b + c, 4 * b - 4 + c, 4 * b - 3 + c
                if kind == "XT":
                    n = (kA + 1) % (B * CPB)
                    n = n if isinstance(b, int) else sp.snap(n)
                    wait(sp, "xt_lo_done", kA + 1)
                    carry()
                    load_xt(n)
                elif kind == "STK":
                    stack_up("k", kA, "k_stacked")
                elif kind == "NRK":
                    stack_norms("k", kA, "k_stacked")
                elif kind == "STQ":
                    stack_up("q", jq, "q_stacked")
                elif kind == "NRQ":
                    stack_norms("q", jq, "q_stacked")
                elif kind == "LX":
                    load_x(b, c, i, j)
                elif kind == "ST":
                    store(b, c, i, j)

            slots(sp, SP_ORDER, step)
            for t in range(TPC):
                sp.wait_ge(stored[t], 16 * B * CPB)
            sp.wait_ge(S["xt_loaded"], 16 * (B * CPB + 1))

        @block.tensor
        def _(pe):
            pe.wait_ge(S["setup"], 1)
            pe.wait_ge(S["pool_const"], 2)

            BANK_USERS = (("KP", "VP", "KN"), ("QP", "QN", "AT", "YT"), ("WO", "FF"))
            FREED = {"KP": ("k_lo", 4), "VP": ("v_lo_done", 4), "KN": ("kn_lo", 1), "QP": ("q_lo", 4),
                     "QN": ("qn_lo", 1), "AT": ("at_lo_done", 4), "YT": ("yt_lo_done", 4),
                     "WO": ("r1_done", 4), "FF": ("r2_done", 4)}

            def bank_free(b, c, kind, i):
                users = next(u for u in BANK_USERS if kind in u)
                mine = [p for p in ENDED if p[0] in users]
                at = next(n for n, p in enumerate(mine) if p[:2] == (kind, i))
                slot = c + mine[at][3]
                for before in range(at - 1, at - 1 - 2 * len(mine), -1):
                    k, n, _, back = mine[before % len(mine)]
                    there = slot + before // len(mine)
                    if runs(b, there, k, back):
                        name, per = FREED[k]
                        wait(pe, name, per * chunk_of(b, there, k, back) + n + 1)
                        return

            def twelve(bank, parts, what, done):
                at = [(kb, s, m) for kb in range(KB) for s, m in (("hi", "hi"), ("lo", "hi"), ("hi", "lo"))]
                for n in (range(0, 6) if what == "first" else range(6, 12)):
                    lhs, rhs = parts(*at[n])
                    last = nc.tensor.matmul(bank[:, :], lhs, rhs, start=n == 0, stop=n == 11)
                if what == "last":
                    last.then_inc(S[done], 1)

            w3, xt_p = {"hi": wqkv_hi, "lo": wqkv_lo}, {"hi": xt_hi, "lo": xt_lo}
            at_p, wo_p = {"hi": at_hi, "lo": at_lo}, {"hi": wout_hi, "lo": wout_lo}
            yt_p, wf_p = [{"hi": yt_hi[:, u, :, :], "lo": yt_lo[:, u, :, :]} for u in range(2)], {"hi": wffn_hi, "lo": wffn_lo}

            def norms(done):
                for g in range(G):
                    last = nc.tensor.matmul(bank_x[32 * g:32 * (g + 1), :] if done == "qn_done" else
                                            bank_a[32 * g:32 * (g + 1), :],
                                            norm_w[:, :], squares[done[0]][:, g, :], start=True, stop=True,
                                            skip_group_check=True)
                last.then_inc(S[done], 1)

            def step(b, c, kind, i, what):
                kA, j, jq = 4 * b + c, 4 * b - 4 + c, 4 * b - 3 + c
                if kind == "KP":
                    if what == "first":
                        if i == 0:
                            wait(pe, "xt_lo_done", kA + 1)
                        bank_free(b, c, kind, i)
                    twelve(bank_a, lambda kb, s, m: (w3[s][:, kb, D + P * i:D + P * (i + 1)],
                                                     xt_p[m][:, c % CPB, kb, :]), what, "kp_done")
                elif kind == "VP":
                    if what == "first":
                        bank_free(b, c, kind, i)
                    twelve(bank_a, lambda kb, s, m: (xt_p[s][:, c % CPB, kb, P * i:P * (i + 1)],
                                                     w3[m][:, kb, 2 * D:3 * D]), what, "vp_done")
                elif kind == "KN":
                    wait(pe, "k_sq", G * (kA + 1))
                    bank_free(b, c, kind, i)
                    norms("kn_done")
                elif kind == "KF":
                    t, g = i // G, i % G
                    if i == 0:
                        wait(pe, "k_stacked", MOVES * (kA + 1))
                    wait(pe, "k_exp", 16 * kA + i)
                    for jj in range(HPG):
                        last = nc.tensor.matmul(bank_kf[:, M * jj:M * (jj + 1)],
                                                stack["k"][0:STACK, jj, g, P * t:P * (t + 1)],
                                                omega_s[0:STACK, :], start=True, stop=True)
                    last.then_inc(S["kf_done"], 1)
                elif kind == "KV":
                    t, g = i // G, i % G
                    if g == 0:
                        wait(pe, "v_lo_done", TPC * kA + t + 1)
                    if i == 0 and c == 0:
                        wait(pe, "kfin", b)
                    wait(pe, "kfl", 16 * kA + i + 1)
                    for jj in range(HPG):
                        h = HPG * g + jj
                        o = kv_ps[h // 8]
                        at = W1 * (h % 8)
                        hi = k_feat_hi[:, i % 2, M * jj:M * (jj + 1)]
                        lo = k_feat_lo[:, i % 2, M * jj:M * (jj + 1)]
                        end = c % CPB == CPB - 1 and t == TPC - 1 and h % 8 == 7
                        nc.tensor.matmul(o[:, at:at + W1], hi, v_hi[:, t, h, :],
                                         start=c == 0 and t == 0 and h % 8 == 0, stop=False,
                                         skip_group_check=True)
                        nc.tensor.matmul(o[:, at:at + DH], hi, v_lo[:, t, h, :], start=False, stop=False,
                                         skip_group_check=True)
                        last = nc.tensor.matmul(o[:, at:at + W1], lo, v_hi[:, t, h, :], start=False,
                                                stop=end, skip_group_check=True)
                    last.then_inc(S["kv_done"], 1)
                elif kind == "QP":
                    if what == "first":
                        bank_free(b, c, kind, i)
                    twelve(bank_x, lambda kb, s, m: (w3[s][:, kb, P * i:P * (i + 1)],
                                                     xt_p[m][:, (c + 1) % CPB, kb, :]), what, "qp_done")
                elif kind == "QN":
                    wait(pe, "q_sq", G * (jq + 1))
                    bank_free(b, c, kind, i)
                    norms("qn_done")
                elif kind == "QF":
                    half, pair = i // 8, i % 8
                    if i == 0:
                        wait(pe, "q_stacked", MOVES * (j + 1))
                    wait(pe, "q_exp", 16 * j + i)
                    for e in range(2):
                        hh = 2 * pair + e
                        last = nc.tensor.matmul(bank_qf[:, HALF * e:HALF * (e + 1)], omega_s[0:STACK, :],
                                                stack["q"][0:STACK, hh // G, hh % G,
                                                           HALF * half:HALF * (half + 1)],
                                                start=True, stop=True)
                    last.then_inc(S["qf_done"], 1)
                elif kind == "NM":
                    t, u = i // 2, i % 2
                    wait(pe, "qfl", 16 * j + 8 * (t // 2 + 1))
                    if i == 0:
                        wait(pe, "kfin", b)
                    wait(pe, "normed", 8 * j + i)
                    for hl in range(8):
                        h = 8 * u + hl
                        hh = G * (h % HPG) + h // HPG
                        pos = slice(P * (t % 2), P * (t % 2 + 1))
                        o = bank_nm[:, W1 * hl:W1 * (hl + 1)]
                        nc.tensor.matmul(o, q_feat_hi[:, hh, pos], kv_hi[:, h, :], start=True, stop=False)
                        nc.tensor.matmul(o, q_feat_hi[:, hh, pos], kv_lo[:, h, :], start=False, stop=False)
                        last = nc.tensor.matmul(o, q_feat_lo[:, hh, pos], kv_hi[:, h, :], start=False,
                                                stop=True)
                    last.then_inc(S["nm_done"], 1)
                elif kind in ("AT", "YT"):
                    if kind == "AT":
                        wait(pe, "normed", 8 * j + 2 * i + 2)
                    else:
                        wait(pe, "y_done", TPC * j + i + 1)
                    bank_free(b, c, kind, i)
                    src = attn[:, :] if kind == "AT" else rows[:, i, :]
                    for kb in range(KB):
                        last = nc.tensor.transpose(bank_x[:, P * kb:P * (kb + 1)],
                                                   src[:, P * kb:P * (kb + 1)], ident[:, :])
                    last.then_inc(S["at_done" if kind == "AT" else "yt_done"], 1)
                elif kind in ("WO", "FF"):
                    if what == "first":
                        wait(pe, "at_lo_done" if kind == "WO" else "yt_lo_done", TPC * j + i + 1)
                        bank_free(b, c, kind, i)
                    l, r = (at_p, wo_p) if kind == "WO" else (yt_p[i % 2], wf_p)
                    twelve(bank_y, lambda kb, s, m: (l[s][:, kb, :], r[m][:, kb, :]), what,
                           "wo_done" if kind == "WO" else "ff_done")

            slots(pe, PE_ORDER, step)

        @block.scalar
        def _(act):
            act.wait_ge(S["setup"], 1)

            def project(s, bank, n, i, first_bias):
                wait(act, f"{s}p_done", G * n + i + 1)
                if i == 0:
                    wait(act, f"{s}_stacked", MOVES * n)
                m = first_bias + i
                nc.scalar.activation(t_hi[s][:, i, :], bank[:, :], ACT.Identity,
                                     bias=bias_qk16[:, m:m + 1]).then_inc(S[f"{s}_hi"], 1)

            def square(s, bank, i, first_bias):
                m = first_bias + i
                nc.scalar.activation(squares[s][:, i, :], bank[:, :], ACT.Square,
                                     bias=bias_qk[:, m:m + 1], scale=1.0 / WS).then_inc(S[f"{s}_sq"], 1)

            def step(b, c, kind, i, what):
                kA, j, jq = 4 * b + c, 4 * b - 4 + c, 4 * b - 3 + c
                if kind == "KP":
                    project("k", bank_a, kA, i, G)
                    if i == 0:
                        wait(act, "kn_done", kA)
                        if c == 1:
                            wait(act, "kfin", b)
                    square("k", bank_a, i, G)
                elif kind == "QP":
                    project("q", bank_x, jq, i, 0)
                    if i == 0:
                        wait(act, "qn_done", jq)
                    square("q", bank_x, i, 0)
                elif kind == "VP":
                    wait(act, "vp_done", TPC * kA + i + 1)
                    if i == 0:
                        wait(act, "kv_done", 16 * kA)
                    nc.scalar.activation(v_hi[:, i, :, 0:DH],
                                         bank_a[:, :].rearrange("p (h d) -> p h d", d=DH),
                                         ACT.Copy).then_inc(S["v_hi_done"], 1)
                elif kind == "KF":
                    wait(act, "kf_done", 16 * kA + i + 1)
                    wait(act, "kv_done", 16 * kA + i - 1)
                    nc.scalar.activation(k_feat[:, i % 2, :], bank_kf[:, :], ACT.Exp,
                                         scale=1.0 / WS).then_inc(S["k_exp"], 1)
                elif kind == "QF":
                    wait(act, "qf_done", 16 * j + i + 1)
                    if i % 8 == 0:
                        wait(act, "nm_done", 8 * j + i // 2)
                    pair = i % 8
                    nc.scalar.activation(q_feat[:, 2 * pair:2 * pair + 2, :],
                                         bank_qf[:, :].rearrange("p (e n) -> p e n", e=2), ACT.Exp,
                                         scale=1.0 / WS).then_inc(S["q_exp"], 1)
                elif kind == "AT":
                    wait(act, "at_done", TPC * j + i + 1)
                    wait(act, "wo_done", TPC * j + i)
                    nc.scalar.activation(at_hi[:, :, :], bank_x[:, :].rearrange("p (k n) -> p k n", k=KB),
                                         ACT.Copy).then_inc(S["at_hi_done"], 1)
                elif kind == "YT":
                    wait(act, "yt_done", TPC * j + i + 1)
                    wait(act, "ff_done", TPC * j + i - 1)
                    nc.scalar.activation(yt_hi[:, i % 2, :, :], bank_x[:, :].rearrange("p (k n) -> p k n", k=KB),
                                         ACT.Copy).then_inc(S["yt_hi_done"], 1)

            slots(act, ACT_ORDER, step)

        @block.vector
        def _(dve):
            v = nc.vector
            v.memset(norm_w[:, :], 0.0).then_inc(S["dve_const"], 1)
            v.memset(minus_half[:, :], -0.5).then_inc(S["dve_const"], 1)
            v.memset(v_hi[:, :, :, DH:W1], 1.0).then_inc(S["dve_const"], 1)
            v.memset(omega_s[96:98, :], WS).then_inc(S["dve_const"], 1)
            dve.wait_ge(S["dve_const"], 4)
            for j in range(HPG):
                v.memset(norm_w[DH * j:DH * (j + 1), j:j + 1], -0.5).then_inc(S["dve_const"], 1)
            dve.wait_ge(S["const_loaded"], 16 * 8)
            v.tensor_copy(omega_s[0:96, :], omega_f[0:96, :]).then_inc(S["dve_const"], 1)
            v.tensor_scalar(bias_qk16[:, :], bias_qk[:, :], WS, None, ALU.mult).then_inc(S["dve_const"], 1)
            v.tensor_scalar(bias_v16[:, :], bias_v16[:, :], WS, None, ALU.mult).then_inc(S["dve_const"], 1)
            dve.wait_ge(S["dve_const"], 11)
            v.tensor_tensor(omega_s[64:96, :], omega_f[64:96, :], omega_s[64:96, :],
                            ALU.subtract).then_inc(S["dve_const"], 1)

            def split_x(slot, k):
                wait(dve, "xt_loaded", 16 * (k + 1))
                v.tensor_copy(xt_hi[:, slot, :, :], xt_f[:, :, :]).then_inc(S["xt_hi_done"], 1)

            for n in range(SETUP_JOBS):
                dve.wait_ge(w_loaded[n % 2], 16 * (n // 2 + 1))
                src = w_stage[:, n % 2, 0:3 * D] if n < KB else w_stage[:, n % 2, :]
                if n < KB:
                    hi, lo = wqkv_hi[:, n, :], wqkv_lo[:, n, :]
                else:
                    hi, lo = (w[:, :, :].rearrange("p k n -> p (k n)")
                              for w in ((wout_hi, wout_lo) if n == KB else (wffn_hi, wffn_lo)))
                if n == KB + 1:
                    for kb in range(KB):
                        last = v.tensor_tensor(src[:, D * kb:D * (kb + 1)], src[:, D * kb:D * (kb + 1)],
                                               attn[:, :], ALU.add).then_inc(S["dve_const"], 1)
                    dve.wait_ge(S["dve_const"], 12 + n + KB)
                v.tensor_scalar(hi, src, WS, None, ALU.mult).then_inc(S["dve_const"], 1)
                dve.wait_ge(S["dve_const"], 12 + n + 1 + (KB if n == KB + 1 else 0))
                v.scalar_tensor_tensor(out=lo, in0=src, scalar=WS, in1=hi, op0=ALU.mult,
                                       op1=ALU.subtract).then_inc(S["w_ready"], 1)
            dve.wait_ge(S["w_ready"], SETUP_JOBS)
            split_x(0, 0)
            v.memset(den[:, :, :], 1.0).then_inc(S["setup"], 1)

            def stats_of(src, ln, u, before, value, s_name, a_name, v_name, n):
                dve.wait_ge(before, value)
                v.bn_stats(stats[:, ln, :], src).then_inc(S[s_name], 1)
                dve.wait_ge(S[s_name], n)
                dve.sem_inc(S["dve_waited"], 1)
                v.bn_aggr(mean_var[:, ln, u, :], stats[:, ln, :]).then_inc(S[a_name], 1)
                dve.wait_ge(S[a_name], n)
                v.tensor_scalar(mean_var[:, ln, u, 1:2], mean_var[:, ln, u, 1:2], LN_EPS, None,
                                ALU.add).then_inc(S[v_name], 1)

            def t_low(s, bank, n, i, first_bias):
                wait(dve, f"{s}_sq", G * n + i + 1)
                if i == 0:
                    wait(dve, f"{s}_stacked", MOVES * n)
                m = first_bias + i
                v.scalar_tensor_tensor(out=t_lo[s][:, i, :], in0=bank[:, :], scalar=bias_qk16[:, m:m + 1],
                                       in1=t_hi[s][:, i, :], op0=ALU.add,
                                       op1=ALU.subtract).then_inc(S[f"{s}_lo"], 1)

            def norm_parts(s, bank, n, k_moved, q_moved):
                wait(dve, f"{s}n_done", n + 1)
                wait(dve, "k_stacked", MOVES * k_moved)
                wait(dve, "q_stacked", MOVES * q_moved)
                v.tensor_scalar(half_norm[:, 0, :], bank[:, :], NORM_MIN, None,
                                ALU.max).then_inc(S[f"{s}n_hi"], 1)
                wait(dve, f"{s}n_hi", n + 1)
                v.scalar_tensor_tensor(out=half_norm[:, 1, :], in0=bank[:, :], scalar=NORM_MIN,
                                       in1=half_norm[:, 0, :], op0=ALU.max,
                                       op1=ALU.subtract).then_inc(S[f"{s}n_lo"], 1)

            def step(b, c, kind, i, what):
                kA, j, jq = 4 * b + c, 4 * b - 4 + c, 4 * b - 3 + c
                n = TPC * j + i + 1
                u = i % 2
                if kind == "KP":
                    t_low("k", bank_a, kA, i, G)
                elif kind == "QP":
                    t_low("q", bank_x, jq, i, 0)
                elif kind == "KN":
                    norm_parts("k", bank_a, kA, kA, jq)
                elif kind == "QN":
                    norm_parts("q", bank_x, jq, min(kA + 1, B * CPB) if isinstance(b, int) else kA + 1, jq)
                elif kind == "VP":
                    wait(dve, "v_hi_done", TPC * kA + i + 1)
                    if i == 0:
                        wait(dve, "kv_done", 16 * kA)
                    v.tensor_tensor(v_lo[:, i, :, :], bank_a[:, :].rearrange("p (h d) -> p h d", d=DH),
                                    v_hi[:, i, :, 0:DH], ALU.subtract).then_inc(S["v_lo_done"], 1)
                elif kind == "KF":
                    wait(dve, "k_exp", 16 * kA + i + 1)
                    wait(dve, "kv_done", 16 * kA + i - 1)
                    v.tensor_tensor(k_feat_lo[:, u, :], k_feat[:, u, :], k_feat_hi[:, u, :],
                                    ALU.subtract).then_inc(S["kfl"], 1)
                elif kind == "QF":
                    wait(dve, "q_exp", 16 * j + i + 1)
                    if i % 8 == 0:
                        wait(dve, "nm_done", 8 * j + i // 2)
                    at = slice(2 * (i % 8), 2 * (i % 8) + 2)
                    v.tensor_tensor(q_feat_lo[:, at, :], q_feat[:, at, :], q_feat_hi[:, at, :],
                                    ALU.subtract).then_inc(S["qfl"], 1)
                elif kind == "KFIN":
                    wait(dve, "kv_done", 16 * (kA + 1))
                    wait(dve, "nm_done", 8 * (j + 1))
                    wait(dve, "kn_done", kA + 2 if runs(b, c + 1, "KN") else kA + 1)
                    for uu in range(2):
                        src = heads(kv_ps[uu])
                        dst = kv_f[:, 8 * uu:8 * uu + 8, :]
                        v.tensor_tensor(dst[:, :, 0:DH],
                                        bias_v16[:, 256 * uu:256 * (uu + 1)].rearrange("p (h d) -> p h d", d=DH),
                                        src[:, :, DH:W1].to_broadcast([P, 8, DH]),
                                        ALU.mult).then_inc(S["fin_a"], 1)
                        v.tensor_copy(dst[:, :, DH:W1], src[:, :, DH:W1]).then_inc(S["fin_a"], 1)
                    done = b + c // CPB
                    wait(dve, "fin_a", 4 * done + 4)
                    for uu in range(2):
                        dst = kv_f[:, 8 * uu:8 * uu + 8, 0:DH]
                        v.tensor_tensor(dst, heads(kv_ps[uu])[:, :, 0:DH], dst, ALU.add).then_inc(S["fin_b"], 1)
                    wait(dve, "fin_b", 2 * done + 2)
                    v.tensor_copy(kv_hi[:, :, :], kv_f[:, :, :]).then_inc(S["fin_c"], 1)
                    wait(dve, "fin_c", done + 1)
                    v.tensor_tensor(kv_lo[:, :, :], kv_f[:, :, :], kv_hi[:, :, :],
                                    ALU.subtract).then_inc(S["kfin"], 1)
                elif kind == "NM":
                    t, uu = i // 2, i % 2
                    m = 8 * j + i + 1
                    wait(dve, "nm_done", m)
                    src = heads(bank_nm)
                    v.tensor_scalar(den[:, 0, :], src[:, :, DH:W1].rearrange("p h o -> p (h o)"), DEN_EPS,
                                    None, ALU.add).then_inc(S["den_done"], 1)
                    wait(dve, "den_done", m)
                    v.reciprocal(den[:, 1, :], den[:, 0, :]).then_inc(S["rec_done"], 1)
                    wait(dve, "rec_done", m)
                    if uu == 0:
                        wait(dve, "at_done", TPC * j + t)
                    v.tensor_tensor(attn[:, 256 * uu:256 * (uu + 1)].rearrange("p (h d) -> p h d", d=DH),
                                    src[:, :, 0:DH],
                                    den[:, 1, :].rearrange("p (h o) -> p h o", o=1).to_broadcast([P, 8, DH]),
                                    ALU.mult).then_inc(S["normed"], 1)
                elif kind == "AT":
                    wait(dve, "at_hi_done", n)
                    v.tensor_tensor(at_lo[:, :, :], bank_x[:, :].rearrange("p (k n) -> p k n", k=KB),
                                    at_hi[:, :, :], ALU.subtract).then_inc(S["at_lo_done"], 1)
                elif kind == "YT":
                    wait(dve, "yt_hi_done", n)
                    v.tensor_tensor(yt_lo[:, u, :, :], bank_x[:, :].rearrange("p (k n) -> p k n", k=KB),
                                    yt_hi[:, u, :, :], ALU.subtract).then_inc(S["yt_lo_done"], 1)
                elif kind == "WO":
                    wait(dve, "wo_done", n)
                    wait(dve, "xb_done", n)
                    v.scalar_tensor_tensor(out=rows[:, i, :], in0=bank_y[:, :], scalar=1.0 / WS / WS,
                                           in1=rows[:, i, :], op0=ALU.mult,
                                           op1=ALU.add).then_inc(S["r1_done"], 1)
                    stats_of(rows[:, i, :], 0, u, S["r1_done"], n, "st1", "ag1", "var1", n)
                elif kind == "Y":
                    wait(dve, "rstd1", n)
                    v.tensor_scalar(rows[:, i, :], rows[:, i, :], mean_var[:, 0, u, 0:1], rstd[:, 0, u:u + 1],
                                    ALU.subtract, ALU.mult).then_inc(S["y_done"], 1)
                elif kind == "FF":
                    wait(dve, "ff_done", n)
                    v.scalar_tensor_tensor(out=rows[:, i, :], in0=bank_y[:, :], scalar=1.0 / WS,
                                           in1=rows[:, i, :], op0=ALU.mult,
                                           op1=ALU.add).then_inc(S["r2_done"], 1)
                    stats_of(rows[:, i, :], 1, u, S["r2_done"], n, "st2", "ag2", "var2", n)
                elif kind == "Z":
                    wait(dve, "rstd2", n)
                    v.tensor_scalar(rows[:, i, :], rows[:, i, :], mean_var[:, 1, u, 0:1], rstd[:, 1, u:u + 1],
                                    ALU.subtract, ALU.mult).then_inc(S["z_done"], 1)
                elif kind == "XS":
                    wait(dve, "qp_done", G * (kA - 2))
                    split_x((c + 1) % CPB, kA + 1)

            slots(dve, DVE_ORDER, step)

        @block.gpsimd
        def _(pool):
            nc.gpsimd.memset(ident[:, :], 0.0).then_inc(S["pool_const"], 1)
            pool.wait_ge(S["pool_const"], 1)
            nc.gpsimd.affine_select(out=ident[:, :], in_=ident[:, :], compare_op=ALU.not_equal, fill=1.0,
                                    base=0, pattern=[[-1, P]], channel_multiplier=1
                                    ).then_inc(S["pool_const"], 1)
            pool.wait_ge(S["dve_const"], 4)
            pool.wait_ge(S["const_loaded"], 16 * 8)

            def split_x_low(slot, k):
                wait(pool, "xt_hi_done", k + 1)
                for kb in range(KB):
                    last = nc.gpsimd.tensor_tensor(xt_lo[:, slot, kb, :], xt_f[:, kb, :],
                                                   xt_hi[:, slot, kb, :], ALU.subtract)
                last.then_inc(S["xt_lo_done"], 1)

            def add_bias(j, t):
                wait(pool, x_loaded[t], 16 * (j + 1))
                nc.gpsimd.tensor_tensor(rows[:, t, :], rows[:, t, :], bias_out[:, :],
                                        ALU.add).then_inc(S["xb_done"], 1)

            split_x_low(0, 0)
            BIAS_BEHIND = (("NM", 0), ("NM", 2), ("QF", 12), ("NM", 4))

            def step(b, c, kind, i, what):
                kA, j = 4 * b + c, 4 * b - 4 + c
                if kind in ("WO", "FF"):
                    ln = 0 if kind == "WO" else 1
                    wait(pool, f"var{ln + 1}", TPC * j + i + 1)
                    nc.gpsimd.tensor_tensor(rstd[:, ln, i % 2:i % 2 + 1], mean_var[:, ln, i % 2, 1:2],
                                            minus_half[:, :], ALU.pow).then_inc(S[f"rstd{ln + 1}"], 1)
                elif (kind, i) in BIAS_BEHIND:
                    add_bias(j, BIAS_BEHIND.index((kind, i)))
                elif kind == "XS":
                    split_x_low((c + 1) % CPB, kA + 1)

            slots(pool, ENDED, step)


_OUT_SHAPE = (B, N, D)


def kernel(**inputs):
    import numpy as _np
    import concourse.bacc as _bacc
    from concourse.bass_utils import run_bass_kernel_spmd as _run

    x = _np.ascontiguousarray(inputs["L0_attn_x"])
    n_chunks, n_tiles = B * N // CHUNK, B * N // P
    bqkv = _np.ascontiguousarray(inputs["L0_attn_bqkv"])
    arrays = {
        "xt": _np.ascontiguousarray(x.reshape(n_chunks, CHUNK, KB, P).transpose(0, 3, 2, 1)),
        "x": x.reshape(n_tiles, P, D),
        "wqkv": _np.ascontiguousarray(inputs["L0_attn_Wqkv"]),
        "bqk": _np.ascontiguousarray(bqkv[:2 * D].reshape(2 * G, P).T),
        "bv": _np.ascontiguousarray(bqkv[2 * D:]),
        "wout": _np.ascontiguousarray(inputs["L0_attn_Wout"]),
        "bout": _np.ascontiguousarray(inputs["L0_attn_bout"]),
        "omega": _np.ascontiguousarray(inputs["L0_attn_omega"]),
        "wffn": _np.ascontiguousarray(_np.asarray(inputs["L0_ffn_weight"]).T),
        "disha": _np.ascontiguousarray(inputs["L0_ffn_disha"]),
    }
    nc = _bacc.Bacc("TRN2", target_bir_lowering=False, num_devices=1)
    args = [nc.dram_tensor(n, a.shape, mybir.dt.from_np(a.dtype), kind="ExternalInput").ap()
            for n, a in arrays.items()]
    out = nc.dram_tensor("out", (n_tiles, P, D), F32, kind="ExternalOutput").ap()
    build(nc, *args, out)
    r = _run(nc, [arrays], core_ids=[0])
    return r.results[0]["out"].reshape(_OUT_SHAPE)
```
